# Optimizing a Trainium2 kernel written in Bass

```python
import numpy as np
import jax
import jax.numpy as jnp

def _softmax(x, axis=-1):
    return jax.nn.softmax(x, axis=axis)

def _gelu(x):
    return jax.nn.gelu(x, approximate=True)

def _silu(x):
    return jax.nn.silu(x)

def _sigmoid(x):
    return jax.nn.sigmoid(x)

def _layernorm(x, axis=-1, eps=1e-05):
    m = jnp.mean(x, axis=axis, keepdims=True)
    v = jnp.var(x, axis=axis, keepdims=True)
    return (x - m) / jnp.sqrt(v + eps)

def _scatter_add(tgt, idx, src, axis=0):
    return tgt.at[idx].add(src)

def _segment_sum(src, seg, n):
    return jax.ops.segment_sum(src, seg, n)
kernel_name = 'mk_dlrm_tower_d1_rec_r8_79b72d'

def setup_inputs(seed: int=0):
    np.random.seed(seed)
    _w = jnp.asarray

    def _rec_inputs():
        import jax
        import jax.numpy as jnp
        _tk = jax.random.key(seed)
        dense_ctx = jax.random.normal(jax.random.fold_in(_tk, 190), (512, 16), jnp.float32)
        ids = jnp.stack([jax.random.randint(jax.random.fold_in(_tk, 200 + f), (512,), 0, v, jnp.int32) for f, v in enumerate([1250, 1250, 1250, 125000, 125000, 12500, 12500, 125000, 125000, 1000, 125000, 12500, 1250, 125000, 12500, 1000, 12500, 1250, 125000, 1000, 1250, 125000, 1000, 125000, 12500, 125000, 125000, 1250, 1250, 12500, 125000, 125000, 1000, 12500, 1250, 1250, 1250, 1000, 125000])], axis=1)
        tbl_0 = 0.05 * jax.random.normal(jax.random.fold_in(_tk, 500 + 0), (1250, 16), jnp.float32)
        tbl_1 = 0.05 * jax.random.normal(jax.random.fold_in(_tk, 500 + 1), (1250, 16), jnp.float32)
        tbl_2 = 0.05 * jax.random.normal(jax.random.fold_in(_tk, 500 + 2), (1250, 16), jnp.float32)
        tbl_3 = 0.05 * jax.random.normal(jax.random.fold_in(_tk, 500 + 3), (125000, 16), jnp.float32)
        tbl_4 = 0.05 * jax.random.normal(jax.random.fold_in(_tk, 500 + 4), (125000, 16), jnp.float32)
        tbl_5 = 0.05 * jax.random.normal(jax.random.fold_in(_tk, 500 + 5), (12500, 16), jnp.float32)
        tbl_6 = 0.05 * jax.random.normal(jax.random.fold_in(_tk, 500 + 6), (12500, 16), jnp.float32)
        tbl_7 = 0.05 * jax.random.normal(jax.random.fold_in(_tk, 500 + 7), (125000, 16), jnp.float32)
        tbl_8 = 0.05 * jax.random.normal(jax.random.fold_in(_tk, 500 + 8), (125000, 16), jnp.float32)
        tbl_9 = 0.05 * jax.random.normal(jax.random.fold_in(_tk, 500 + 9), (1000, 16), jnp.float32)
        tbl_10 = 0.05 * jax.random.normal(jax.random.fold_in(_tk, 500 + 10), (125000, 16), jnp.float32)
        tbl_11 = 0.05 * jax.random.normal(jax.random.fold_in(_tk, 500 + 11), (12500, 16), jnp.float32)
        tbl_12 = 0.05 * jax.random.normal(jax.random.fold_in(_tk, 500 + 12), (1250, 16), jnp.float32)
        tbl_13 = 0.05 * jax.random.normal(jax.random.fold_in(_tk, 500 + 13), (125000, 16), jnp.float32)
        tbl_14 = 0.05 * jax.random.normal(jax.random.fold_in(_tk, 500 + 14), (12500, 16), jnp.float32)
        tbl_15 = 0.05 * jax.random.normal(jax.random.fold_in(_tk, 500 + 15), (1000, 16), jnp.float32)
        tbl_16 = 0.05 * jax.random.normal(jax.random.fold_in(_tk, 500 + 16), (12500, 16), jnp.float32)
        tbl_17 = 0.05 * jax.random.normal(jax.random.fold_in(_tk, 500 + 17), (1250, 16), jnp.float32)
        tbl_18 = 0.05 * jax.random.normal(jax.random.fold_in(_tk, 500 + 18), (125000, 16), jnp.float32)
        tbl_19 = 0.05 * jax.random.normal(jax.random.fold_in(_tk, 500 + 19), (1000, 16), jnp.float32)
        tbl_20 = 0.05 * jax.random.normal(jax.random.fold_in(_tk, 500 + 20), (1250, 16), jnp.float32)
        tbl_21 = 0.05 * jax.random.normal(jax.random.fold_in(_tk, 500 + 21), (125000, 16), jnp.float32)
        tbl_22 = 0.05 * jax.random.normal(jax.random.fold_in(_tk, 500 + 22), (1000, 16), jnp.float32)
        tbl_23 = 0.05 * jax.random.normal(jax.random.fold_in(_tk, 500 + 23), (125000, 16), jnp.float32)
        tbl_24 = 0.05 * jax.random.normal(jax.random.fold_in(_tk, 500 + 24), (12500, 16), jnp.float32)
        tbl_25 = 0.05 * jax.random.normal(jax.random.fold_in(_tk, 500 + 25), (125000, 16), jnp.float32)
        tbl_26 = 0.05 * jax.random.normal(jax.random.fold_in(_tk, 500 + 26), (125000, 16), jnp.float32)
        tbl_27 = 0.05 * jax.random.normal(jax.random.fold_in(_tk, 500 + 27), (1250, 16), jnp.float32)
        tbl_28 = 0.05 * jax.random.normal(jax.random.fold_in(_tk, 500 + 28), (1250, 16), jnp.float32)
        tbl_29 = 0.05 * jax.random.normal(jax.random.fold_in(_tk, 500 + 29), (12500, 16), jnp.float32)
        tbl_30 = 0.05 * jax.random.normal(jax.random.fold_in(_tk, 500 + 30), (125000, 16), jnp.float32)
        tbl_31 = 0.05 * jax.random.normal(jax.random.fold_in(_tk, 500 + 31), (125000, 16), jnp.float32)
        tbl_32 = 0.05 * jax.random.normal(jax.random.fold_in(_tk, 500 + 32), (1000, 16), jnp.float32)
        tbl_33 = 0.05 * jax.random.normal(jax.random.fold_in(_tk, 500 + 33), (12500, 16), jnp.float32)
        tbl_34 = 0.05 * jax.random.normal(jax.random.fold_in(_tk, 500 + 34), (1250, 16), jnp.float32)
        tbl_35 = 0.05 * jax.random.normal(jax.random.fold_in(_tk, 500 + 35), (1250, 16), jnp.float32)
        tbl_36 = 0.05 * jax.random.normal(jax.random.fold_in(_tk, 500 + 36), (1250, 16), jnp.float32)
        tbl_37 = 0.05 * jax.random.normal(jax.random.fold_in(_tk, 500 + 37), (1000, 16), jnp.float32)
        tbl_38 = 0.05 * jax.random.normal(jax.random.fold_in(_tk, 500 + 38), (125000, 16), jnp.float32)
        _rk = jax.random.fold_in(_tk, 7)
        W_top1 = 0.0606339 * jax.random.normal(jax.random.fold_in(_tk, 801), (272, 512), jnp.float32)
        W_top2 = 0.0441942 * jax.random.normal(jax.random.fold_in(_tk, 802), (512, 256), jnp.float32)
        W_top3 = 0.0625 * jax.random.normal(jax.random.fold_in(_tk, 803), (256, 1), jnp.float32)
        b_top1 = jnp.zeros((512,), jnp.float32)
        b_top2 = jnp.zeros((256,), jnp.float32)
        return (dense_ctx, ids, tbl_0, tbl_1, tbl_2, tbl_3, tbl_4, tbl_5, tbl_6, tbl_7, tbl_8, tbl_9, tbl_10, tbl_11, tbl_12, tbl_13, tbl_14, tbl_15, tbl_16, tbl_17, tbl_18, tbl_19, tbl_20, tbl_21, tbl_22, tbl_23, tbl_24, tbl_25, tbl_26, tbl_27, tbl_28, tbl_29, tbl_30, tbl_31, tbl_32, tbl_33, tbl_34, tbl_35, tbl_36, tbl_37, tbl_38, W_top1, b_top1, W_top2, b_top2, W_top3)
    dense_ctx, ids, tbl_0, tbl_1, tbl_2, tbl_3, tbl_4, tbl_5, tbl_6, tbl_7, tbl_8, tbl_9, tbl_10, tbl_11, tbl_12, tbl_13, tbl_14, tbl_15, tbl_16, tbl_17, tbl_18, tbl_19, tbl_20, tbl_21, tbl_22, tbl_23, tbl_24, tbl_25, tbl_26, tbl_27, tbl_28, tbl_29, tbl_30, tbl_31, tbl_32, tbl_33, tbl_34, tbl_35, tbl_36, tbl_37, tbl_38, W_top1, b_top1, W_top2, b_top2, W_top3 = _rec_inputs()

    def _L0_rec_setup():
        import jax, jax.numpy as jnp
        import numpy as np
        key = jax.random.key(seed)
        k1, k2, k3 = jax.random.split(key, 3)
        B, M, D = (512, 39, 16)
        H = [128, 128]
        x = jax.random.normal(k1, (B, M, D), dtype=jnp.float32)
        W0 = jax.random.normal(k2, (1, M * M, H[0]), dtype=jnp.float32) * 0.05
        W1 = jax.random.normal(k3, (1, M * H[0], H[1]), dtype=jnp.float32) * 0.05
        return {'x': x, 'W0': W0, 'W1': W1}
    _L0_rec_all = _L0_rec_setup()
    _L0_rec_in = {k: v for k, v in _L0_rec_all.items() if k in ('W0', 'W1')}
    del _L0_rec_all
    return {'dense_ctx': dense_ctx, 'ids': ids, 'tbl_0': tbl_0, 'tbl_1': tbl_1, 'tbl_2': tbl_2, 'tbl_3': tbl_3, 'tbl_4': tbl_4, 'tbl_5': tbl_5, 'tbl_6': tbl_6, 'tbl_7': tbl_7, 'tbl_8': tbl_8, 'tbl_9': tbl_9, 'tbl_10': tbl_10, 'tbl_11': tbl_11, 'tbl_12': tbl_12, 'tbl_13': tbl_13, 'tbl_14': tbl_14, 'tbl_15': tbl_15, 'tbl_16': tbl_16, 'tbl_17': tbl_17, 'tbl_18': tbl_18, 'tbl_19': tbl_19, 'tbl_20': tbl_20, 'tbl_21': tbl_21, 'tbl_22': tbl_22, 'tbl_23': tbl_23, 'tbl_24': tbl_24, 'tbl_25': tbl_25, 'tbl_26': tbl_26, 'tbl_27': tbl_27, 'tbl_28': tbl_28, 'tbl_29': tbl_29, 'tbl_30': tbl_30, 'tbl_31': tbl_31, 'tbl_32': tbl_32, 'tbl_33': tbl_33, 'tbl_34': tbl_34, 'tbl_35': tbl_35, 'tbl_36': tbl_36, 'tbl_37': tbl_37, 'tbl_38': tbl_38, 'W_top1': W_top1, 'b_top1': b_top1, 'W_top2': W_top2, 'b_top2': b_top2, 'W_top3': W_top3, 'L0_rec_W0': _L0_rec_in['W0'], 'L0_rec_W1': _L0_rec_in['W1']}

def reference(dense_ctx, ids, tbl_0, tbl_1, tbl_2, tbl_3, tbl_4, tbl_5, tbl_6, tbl_7, tbl_8, tbl_9, tbl_10, tbl_11, tbl_12, tbl_13, tbl_14, tbl_15, tbl_16, tbl_17, tbl_18, tbl_19, tbl_20, tbl_21, tbl_22, tbl_23, tbl_24, tbl_25, tbl_26, tbl_27, tbl_28, tbl_29, tbl_30, tbl_31, tbl_32, tbl_33, tbl_34, tbl_35, tbl_36, tbl_37, tbl_38, W_top1, b_top1, W_top2, b_top2, W_top3, L0_rec_W0, L0_rec_W1):
    import jax
    import jax.numpy as jnp

    def _L0_rec_ref(x, W0, W1):
        import jax, jax.numpy as jnp
        import numpy as np
        m = x.shape[1]
        x0 = x
        xk = x
        outs = []
        for W in (W0, W1):
            Hk = xk.shape[1]
            Hn = W.shape[-1]
            Wr = W.reshape(m, Hk, Hn)
            xk = jnp.einsum('bid,bjd,ijh->bhd', x0, xk, Wr)
            outs.append(xk)
        result = jnp.concatenate(outs, axis=1)
        return jnp.sum(result, axis=-1)
    e = jnp.stack([tbl_0[ids[:, 0]], tbl_1[ids[:, 1]], tbl_2[ids[:, 2]], tbl_3[ids[:, 3]], tbl_4[ids[:, 4]], tbl_5[ids[:, 5]], tbl_6[ids[:, 6]], tbl_7[ids[:, 7]], tbl_8[ids[:, 8]], tbl_9[ids[:, 9]], tbl_10[ids[:, 10]], tbl_11[ids[:, 11]], tbl_12[ids[:, 12]], tbl_13[ids[:, 13]], tbl_14[ids[:, 14]], tbl_15[ids[:, 15]], tbl_16[ids[:, 16]], tbl_17[ids[:, 17]], tbl_18[ids[:, 18]], tbl_19[ids[:, 19]], tbl_20[ids[:, 20]], tbl_21[ids[:, 21]], tbl_22[ids[:, 22]], tbl_23[ids[:, 23]], tbl_24[ids[:, 24]], tbl_25[ids[:, 25]], tbl_26[ids[:, 26]], tbl_27[ids[:, 27]], tbl_28[ids[:, 28]], tbl_29[ids[:, 29]], tbl_30[ids[:, 30]], tbl_31[ids[:, 31]], tbl_32[ids[:, 32]], tbl_33[ids[:, 33]], tbl_34[ids[:, 34]], tbl_35[ids[:, 35]], tbl_36[ids[:, 36]], tbl_37[ids[:, 37]], tbl_38[ids[:, 38]]], axis=1)
    z = _L0_rec_ref(e, L0_rec_W0, L0_rec_W1)
    z = z.reshape(z.shape[0], -1)
    h = jnp.concatenate([z, dense_ctx], axis=1)
    h = jnp.maximum(h @ W_top1 + b_top1, 0.0)
    h = jnp.maximum(h @ W_top2 + b_top2, 0.0)
    y = h @ W_top3
    return y

_drawn_inputs = setup_inputs


def setup_inputs(seed=0):
    import zlib

    import numpy as np

    out = dict(_drawn_inputs(seed))
    spreads = {'b_top1': (0.0, 0.1), 'b_top2': (0.0, 0.1)}
    factors = {'tbl_0': 4.765,
     'tbl_1': 5.311,
     'tbl_2': 4.83,
     'tbl_3': 5.154,
     'tbl_4': 5.263,
     'tbl_5': 4.907,
     'tbl_6': 4.632,
     'tbl_7': 4.895,
     'tbl_8': 4.957,
     'tbl_9': 4.667,
     'tbl_10': 5.276,
     'tbl_11': 4.99,
     'tbl_12': 4.382,
     'tbl_13': 4.314,
     'tbl_14': 4.92,
     'tbl_15': 4.891,
     'tbl_16': 5.373,
     'tbl_17': 5.271,
     'tbl_18': 5.548,
     'tbl_19': 5.353,
     'tbl_20': 4.9,
     'tbl_21': 5.267,
     'tbl_22': 4.79,
     'tbl_23': 5.071,
     'tbl_24': 4.601,
     'tbl_25': 4.583,
     'tbl_26': 5.145,
     'tbl_27': 5.038,
     'tbl_28': 5.203,
     'tbl_29': 4.801,
     'tbl_30': 4.974,
     'tbl_31': 4.852,
     'tbl_32': 5.105,
     'tbl_33': 5.074,
     'tbl_34': 4.931,
     'tbl_35': 4.972,
     'tbl_36': 5.117,
     'tbl_37': 5.217,
     'tbl_38': 5.192,
     'L0_rec_W1': 5.506}
    for name, (base, spread) in spreads.items():
        noise = np.random.default_rng([zlib.crc32(name.encode()), seed]).standard_normal(out[name].shape)
        drawn = base * np.exp(spread * noise) if base else spread * noise
        out[name] = jnp.asarray(drawn.astype(out[name].dtype))
    for name, factor in factors.items():
        out[name] = (out[name] * factor).astype(out[name].dtype)
    return out
```

```python
from contextlib import ExitStack

import numpy as np

import concourse.bass as bass
from concourse import mybir

F32 = mybir.dt.float32
F32R = mybir.dt.float32r
I32 = mybir.dt.int32
ALU = mybir.AluOpType
ACT = mybir.ActivationFunctionType

P = 128
B = 512
M = 39
D = 16
H = 128
TILES = B // P
BLOCKS = 4
COLS = P * D // BLOCKS
SB = P // BLOCKS
GROUPS = 4
SG = P // D
NPAIRS = M * (M + 1) // 2
CHUNKS = -(-NPAIRS // P)
LAST = CHUNKS - 1
REST = NPAIRS - LAST * P
AT_HH, AT_HL, AT_LH = 0, 32, 64
LAST_ROWS = AT_LH + REST
TC = BLOCKS * CHUNKS
GI = M + 1
ROWS = 2 * M + 1
NP, NS = 2, 4
H1C, H2C = 4, 2
HI_ON_ACT = (0, 2, 4, 6)


def rows_of(c):
    return P if c < LAST else LAST_ROWS


def on_act(g):
    return g // CHUNKS * len(HI_ON_ACT) + sum(c <= g % CHUNKS for c in HI_ON_ACT)


def on_dve(g):
    return g + 1 - on_act(g)


ACT_TILE = on_act(TC - 1)
DVE_TILE = on_dve(TC - 1)


def build(nc, tables, ids, dense_t, w0_pairs, w1, wt1, bt1, wt2, bt2, wt3,
          sel_c, inc_c, ident_c, out):
    with ExitStack() as ctx:
        def sb(name, shape, dt=F32):
            return ctx.enter_context(nc.sbuf_tensor(name, shape, dt))

        def ps(name, shape):
            return ctx.enter_context(nc.psum_tensor(name, shape, F32))

        def sem(name):
            return ctx.enter_context(nc.semaphore(name))

        idx = sb("idx", [P, TILES * M], I32)
        emb = sb("emb", [P, TILES, M * D])
        split = sb("split", [P, D, 2 * GI])
        xt = sb("xt", [ROWS, P * D], F32R)
        squares = sb("squares", [P, NP, COLS])
        sq_hi = sb("sq_hi", [P, NS, COLS], F32R)
        sq_lo = sb("sq_lo", [P, NS, COLS], F32R)
        xk = sb("xk", [H, COLS])
        xkt_hi = sb("xkt_hi", [P, GROUPS, H], F32R)
        xkt_lo = sb("xkt_lo", [P, GROUPS, H], F32R)
        xdiag = sb("xdiag", [P, BLOCKS * GROUPS, SG, 2 * GI], F32R)
        gs = sb("gs", [H, GI, P])
        zt = sb("zt", [H, 2, P])
        hid1 = sb("hid1", [P, H1C, P])
        hid2 = sb("hid2", [P, H2C, P])
        yrow = sb("yrow", [1, B])
        dense_sb = sb("dense_sb", [D, B])
        w0u = sb("w0u", [P, CHUNKS, H])
        w0l = sb("w0l", [P, CHUNKS, H])
        w0sum = sb("w0sum", [P, CHUNKS, H])
        w0 = sb("w0", [P, CHUNKS, H])
        w0_hi = sb("w0_hi", [P, CHUNKS, H], F32R)
        w0_lo = sb("w0_lo", [P, CHUNKS, H], F32R)
        w1_sb = sb("w1_sb", [H, M, H])
        wt1_sb = sb("wt1_sb", [P, 2, H1C * P])
        wt1d_sb = sb("wt1d_sb", [D, H1C * P])
        wt2_sb = sb("wt2_sb", [P, H1C, H2C * P])
        wt3_sb = sb("wt3_sb", [P, H2C])
        bt1_sb = sb("bt1_sb", [P, H1C])
        bt2_sb = sb("bt2_sb", [P, H2C])
        sel_f = sb("sel_f", [ROWS, CHUNKS * P])
        sel = sb("sel", [ROWS, CHUNKS, P], F32R)
        inc = sb("inc", [P, CHUNKS, M])
        ident = sb("ident", [P, P])
        spill = nc.dram_tensor("spill", [P, D, 2 * GI], F32).ap()

        sums = ps("sums", [P, 2, COLS])
        acc = ps("acc", [P, COLS])
        misc = ps("misc", [P, COLS])
        gp = ps("gp", [P, GROUPS, COLS])

        ids_in = sem("ids_in")
        consts_in = sem("consts_in")
        w0_in = sem("w0_in")
        w1_in = sem("w1_in")
        mlp_in = sem("mlp_in")
        rows_in = [sem(f"rows_in{t}") for t in range(TILES)]
        tile_gathered = sem("tile_gathered")
        edges_set = sem("edges_set")
        sel_cast = sem("sel_cast")
        w0_summed = sem("w0_summed")
        w0_halved = sem("w0_halved")
        diag_summed = sem("diag_summed")
        w0_ready = sem("w0_ready")
        xdiag_clear = sem("xdiag_clear")
        hi_split = sem("hi_split")
        emb_split = sem("emb_split")
        spilled = sem("spilled")
        spread = sem("spread")
        emb_turned = sem("emb_turned")
        xt_by_dve = sem("xt_by_dve")
        xt_by_act = sem("xt_by_act")
        sum_ready = sem("sum_ready")
        squared = sem("squared")
        hi_by_act = sem("hi_by_act")
        hi_by_dve = sem("hi_by_dve")
        lo_ready = sem("lo_ready")
        chunk_used = sem("chunk_used")
        xk_copied = sem("xk_copied")
        xk_turned = sem("xk_turned")
        xkt_hi_ready = sem("xkt_hi_ready")
        xkt_lo_ready = sem("xkt_lo_ready")
        g_ready = sem("g_ready")
        g_copied = sem("g_copied")
        z2_ready = sem("z2_ready")
        z_copied = sem("z_copied")
        h1_ready = sem("h1_ready")
        h1_done = sem("h1_done")
        h2_ready = sem("h2_ready")
        h2_done = sem("h2_done")
        y_ready = sem("y_ready")
        y_copied = sem("y_copied")
        y_out = sem("y_out")

        xt_v = xt[:, :].rearrange("r (b d) -> r b d", d=D)
        emb_v = emb[:, :, :].rearrange("p t (f d) -> p t d f", d=D)
        xkt_hi_flat = xkt_hi[:, :, :].rearrange("p k h -> p (k h)")
        xkt_lo_flat = xkt_lo[:, :, :].rearrange("p k h -> p (k h)")
        turn_banks = [sums[:, 0, :], sums[:, 1, :], acc[:, :], sums[:, 0, :]]

        block = ctx.enter_context(nc.Block())

        @block.sync
        def _(sp):
            sp.dma_start(idx[:, :], ids).then_inc(ids_in, 16)
            sp.dma_start(w0u[:, :, :], w0_pairs[0]).then_inc(w0_in, 16)
            sp.dma_start(w0l[:, :, :], w0_pairs[1]).then_inc(w0_in, 16)
            sp.dma_start(w1_sb[:, :, :], w1).then_inc(w1_in, 16)
            sp.dma_start(wt1_sb[:, :, :], wt1[0:2 * H, :].rearrange("(k p) n -> p k n", p=P)).then_inc(mlp_in, 16)
            sp.dma_start(wt1d_sb[:, :], wt1[2 * H:2 * H + D, :]).then_inc(mlp_in, 16)
            sp.dma_start(wt2_sb[:, :, :], wt2.rearrange("(k p) n -> p k n", p=P)).then_inc(mlp_in, 16)
            sp.dma_start(wt3_sb[:, :], wt3).then_inc(mlp_in, 16)
            sp.dma_start(bt1_sb[:, :], bt1).then_inc(mlp_in, 16)
            sp.dma_start(bt2_sb[:, :], bt2).then_inc(mlp_in, 16)
            sp.dma_start(dense_sb[:, :], dense_t).then_inc(mlp_in, 16)
            for t in range(TILES):
                sp.wait_ge(rows_in[t], 16 * M)
                sp.sem_inc(tile_gathered, 1)
                sp.wait_ge(emb_split, t + 1)
                if t > 0:
                    sp.wait_ge(spread, 16 * SG * t)
                sp.dma_start(spill, split[:, :, :]).then_inc(spilled, 16)
                sp.wait_ge(spilled, 16 * (t + 1))
                if t == 0:
                    sp.wait_ge(xdiag_clear, 1)
                else:
                    sp.wait_ge(g_ready, BLOCKS * t)
                for e in range(SG):
                    sp.dma_start(xdiag[e * D:(e + 1) * D, :, e, :].bitcast(F32),
                                 spill.rearrange("(g e) d r -> e d g r", e=SG)[e]).then_inc(spread, 16)
            sp.wait_ge(y_copied, TILES)
            sp.dma_start(out, yrow[:, :]).then_inc(y_out, 16)
            sp.wait_ge(y_out, 16)

        @block.gpsimd
        def _(pool):
            pool.wait_ge(ids_in, 16)
            for t in range(TILES):
                for f in range(M):
                    pool.indirect_dma_start(
                        out=emb[:, t, f * D:(f + 1) * D], out_offset=None, in_=tables[f],
                        in_offset=bass.IndirectOffsetOnAxis(ap=idx[:, t * M + f:t * M + f + 1], axis=0),
                    ).then_inc(rows_in[t], 16)

        @block.scalar
        def _(act):
            act.dma_start(ident[:, :], ident_c).then_inc(consts_in, 16)
            act.dma_start(sel_f[:, :], sel_c).then_inc(consts_in, 16)
            act.dma_start(inc[:, :, :], inc_c).then_inc(consts_in, 16)

            def turned_xk_hi(b):
                act.wait_ge(xk_turned, b + 1)
                nc.scalar.copy(xkt_hi_flat, misc[:, :]).then_inc(xkt_hi_ready, 1)

            def tile(t, first):
                if not first:
                    turned_xk_hi(BLOCKS * t - 1)
                for m in (1, 3):
                    act.wait_ge(emb_turned, 4 * t + m + 1)
                    nc.scalar.copy(xt_v[:, :, 4 * m:4 * m + 4],
                                   turn_banks[m][0:ROWS, :].rearrange("r (d b) -> r b d", d=4)).then_inc(xt_by_act, 1)
                for g in range(TC):
                    n, c = divmod(g, CHUNKS)
                    r = rows_of(c)
                    act.wait_ge(sum_ready, TC * t + g + 1)
                    if not first or g >= NP:
                        act.wait_ge(lo_ready, TC * t + g + 1 - NP)
                    nc.scalar.activation(squares[0:r, g % NP, :], sums[0:r, g % 2, :],
                                         ACT.Square).then_inc(squared, 1)
                    if c in HI_ON_ACT:
                        if not first or g >= NS:
                            act.wait_ge(chunk_used, TC * t + g + 1 - NS)
                        nc.scalar.activation(sq_hi[0:r, g % NS, :], sums[0:r, g % 2, :],
                                             ACT.Square).then_inc(hi_by_act, 1)
                    if n > 0 and c == 3:
                        turned_xk_hi(BLOCKS * t + n - 1)

            tile(0, True)
            with act.Fori(1, TILES) as t:
                tile(t, False)
            turned_xk_hi(BLOCKS * TILES - 1)

        @block.vector
        def _(dve):
            nc.vector.memset(split[:, :, M:M + 1], 1.0)
            nc.vector.memset(split[:, :, 2 * GI - 1:2 * GI], 0.0).then_inc(edges_set, 1)
            dve.wait_ge(consts_in, 3 * 16)
            nc.vector.tensor_copy(sel[:, :, :].rearrange("r c p -> r (c p)"), sel_f[:, :]).then_inc(sel_cast, 1)
            dve.wait_ge(w0_in, 2 * 16)
            nc.vector.tensor_tensor(w0sum[:, :, :], w0u[:, :, :], w0l[:, :, :], ALU.add).then_inc(w0_summed, 1)
            dve.wait_ge(w0_summed, 1)
            nc.vector.tensor_scalar(w0[:, :, :], w0sum[:, :, :], 0.5, None, ALU.mult).then_inc(w0_halved, 1)
            dve.wait_ge(diag_summed, 1)
            dve.wait_ge(w0_halved, 1)
            nc.vector.tensor_copy(w0[0:M, 0, :], misc[0:M, 0:H]).then_inc(w0_halved, 1)
            dve.wait_ge(w0_halved, 2)
            nc.vector.tensor_copy(w0_hi[:, :, :], w0[:, :, :]).then_inc(w0_ready, 1)
            dve.wait_ge(w0_ready, 1)
            nc.vector.tensor_tensor(w0_lo[:, :, :], w0[:, :, :], w0_hi[:, :, :].bitcast(F32),
                                    ALU.subtract).then_inc(w0_ready, 1)
            dve.wait_ge(w0_ready, 2)
            nc.vector.tensor_copy(w0_hi[AT_LH:LAST_ROWS, LAST, :],
                                  w0_lo[AT_LH:LAST_ROWS, LAST, :].bitcast(F32)).then_inc(w0_ready, 1)
            nc.vector.memset(xdiag[:, :, :, :].bitcast(F32), 0.0).then_inc(xdiag_clear, 1)

            def parts(t, first, g):
                c = g % CHUNKS
                r = rows_of(c)
                dve.wait_ge(squared, TC * t + g + 1)
                if not first or g >= NS:
                    dve.wait_ge(chunk_used, TC * t + g + 1 - NS)
                if c in HI_ON_ACT:
                    dve.wait_ge(hi_by_act, ACT_TILE * t + on_act(g))
                else:
                    nc.vector.tensor_copy(sq_hi[0:r, g % NS, :], squares[0:r, g % NP, :]).then_inc(hi_by_dve, 1)
                    dve.wait_ge(hi_by_dve, DVE_TILE * t + on_dve(g))
                if c < LAST:
                    rows, lo = slice(0, P), sq_lo
                else:
                    rows, lo = slice(AT_HL, AT_HL + REST), sq_hi
                nc.vector.tensor_tensor(lo[rows, g % NS, :], squares[rows, g % NP, :],
                                        sq_hi[rows, g % NS, :].bitcast(F32), ALU.subtract).then_inc(lo_ready, 1)

            def turned_xk_lo(b):
                dve.wait_ge(xk_turned, b + 1)
                dve.wait_ge(xkt_hi_ready, b + 1)
                nc.vector.tensor_tensor(xkt_lo_flat, misc[:, :], xkt_hi_flat.bitcast(F32),
                                        ALU.subtract).then_inc(xkt_lo_ready, 1)

            def copy_xk(b):
                dve.wait_ge(chunk_used, CHUNKS * (b + 1))
                nc.vector.tensor_copy(xk[:, :], acc[:, :]).then_inc(xk_copied, 1)

            def copy_g(b, n):
                dve.wait_ge(g_ready, b + 1)
                nc.vector.tensor_copy(
                    gs[:, :, n * SB:(n + 1) * SB].rearrange("h i (k e) -> h k e i", k=GROUPS),
                    gp[:, :, 0:SG * GI].rearrange("h k (e i) -> h k e i", e=SG)).then_inc(g_copied, 1)

            def copy_z(t):
                dve.wait_ge(z2_ready, t + 1)
                nc.vector.tensor_copy(zt[:, 0, :], gs[:, M, :])
                nc.vector.tensor_copy(zt[:, 1, :], misc[:, 0:P]).then_inc(z_copied, 1)

            def relu1(t):
                dve.wait_ge(h1_ready, t + 1)
                for m in range(H1C):
                    last = nc.vector.tensor_scalar(hid1[:, m, :], misc[:, m * P:(m + 1) * P],
                                                   bt1_sb[:, m:m + 1], 0.0, ALU.add, ALU.max)
                last.then_inc(h1_done, 1)

            def relu2(t):
                dve.wait_ge(h2_ready, t + 1)
                for m in range(H2C):
                    last = nc.vector.tensor_scalar(hid2[:, m, :], misc[:, m * P:(m + 1) * P],
                                                   bt2_sb[:, m:m + 1], 0.0, ALU.add, ALU.max)
                last.then_inc(h2_done, 1)

            def copy_y(t):
                dve.wait_ge(y_ready, t + 1)
                nc.vector.tensor_copy(yrow[:, bass.ts(t, P)], misc[0:1, 0:P]).then_inc(y_copied, 1)

            def split_emb(t, first):
                dve.wait_ge(tile_gathered, t + 1)
                if not first:
                    dve.wait_ge(emb_turned, 4 * t)
                    dve.wait_ge(spilled, 16 * t)
                e = emb_v[:, t, :, :] if first else emb_v[:, bass.ds(t, 1), :, :].rearrange("p o d f -> p (o d) f")
                nc.vector.tensor_copy(split[:, :, 0:M].bitcast(F32R), e).then_inc(hi_split, 1)
                dve.wait_ge(hi_split, t + 1)
                nc.vector.tensor_tensor(split[:, :, GI:GI + M], e, split[:, :, 0:M], ALU.subtract).then_inc(emb_split, 1)

            def tile(t, first):
                split_emb(t, first)
                if not first:
                    copy_g(BLOCKS * t - 2, BLOCKS - 2)
                    turned_xk_lo(BLOCKS * t - 1)
                for m in (0, 2):
                    dve.wait_ge(emb_turned, 4 * t + m + 1)
                    nc.vector.tensor_copy(xt_v[:, :, 4 * m:4 * m + 4],
                                          turn_banks[m][0:ROWS, :].rearrange("r (d b) -> r b d", d=4)).then_inc(xt_by_dve, 1)
                if not first:
                    copy_g(BLOCKS * t - 1, BLOCKS - 1)
                for g in range(TC):
                    n, c = divmod(g, CHUNKS)
                    b = BLOCKS * t + n
                    parts(t, first, g)
                    if c == 0:
                        if n == 1 and not first:
                            relu1(t - 1)
                        if n >= 2:
                            copy_g(b - 2, n - 2)
                            if not first:
                                (relu2, copy_y)[n - 2](t - 1)
                    if c == 3 and n > 0:
                        turned_xk_lo(b - 1)
                    if c == 4 and n == 0 and not first:
                        copy_z(t - 1)
                    if c == LAST:
                        copy_xk(b)

            dve.wait_ge(mlp_in, 7 * 16)
            tile(0, True)
            with dve.Fori(1, TILES) as t:
                tile(t, False)
            copy_g(BLOCKS * TILES - 2, BLOCKS - 2)
            turned_xk_lo(BLOCKS * TILES - 1)
            copy_g(BLOCKS * TILES - 1, BLOCKS - 1)
            copy_z(TILES - 1)
            relu1(TILES - 1)
            relu2(TILES - 1)
            copy_y(TILES - 1)

        @block.tensor
        def _(pe):
            pe.wait_ge(consts_in, 3 * 16)
            pe.wait_ge(w0_summed, 1)
            for c in range(CHUNKS):
                r = P if c < LAST else REST
                last = nc.tensor.matmul(misc[0:M, 0:H], inc[0:r, c, :], w0sum[0:r, c, :],
                                        start=(c == 0), stop=(c == CHUNKS - 1))
            last.then_inc(diag_summed, 1)
            pe.wait_ge(sel_cast, 1)
            pe.wait_ge(edges_set, 1)

            def turn_emb(t, m):
                for d in range(4):
                    last = nc.tensor.transpose(turn_banks[m][0:ROWS, d * P:(d + 1) * P],
                                               split[:, 4 * m + d, 0:ROWS], ident[:, :])
                last.then_inc(emb_turned, 1)

            def pair_sums(t, first, g):
                n, c = divmod(g, CHUNKS)
                r = rows_of(c)
                if g >= 2:
                    pe.wait_ge(squared, TC * t + g - 1)
                    if (g - 2) % CHUNKS in HI_ON_ACT:
                        pe.wait_ge(hi_by_act, ACT_TILE * t + on_act(g - 2))
                nc.tensor.matmul(sums[0:r, g % 2, :], sel[:, c, 0:r], xt[:, n * COLS:(n + 1) * COLS],
                                 start=True, stop=True).then_inc(sum_ready, 1)

            def layer1(t, first, g):
                n, c = divmod(g, CHUNKS)
                r = rows_of(c)
                if c in HI_ON_ACT:
                    pe.wait_ge(hi_by_act, ACT_TILE * t + on_act(g))
                else:
                    pe.wait_ge(hi_by_dve, DVE_TILE * t + on_dve(g))
                if c == 0 and (n > 0 or not first):
                    pe.wait_ge(xk_copied, BLOCKS * t + n)
                if c < LAST:
                    nc.tensor.matmul(acc[:, :], w0_hi[0:r, c, :], sq_hi[0:r, g % NS, :], start=(c == 0), stop=False)
                    nc.tensor.matmul(acc[:, :], w0_lo[0:r, c, :], sq_hi[0:r, g % NS, :], start=False, stop=False)
                    pe.wait_ge(lo_ready, TC * t + g + 1)
                    last = nc.tensor.matmul(acc[:, :], w0_hi[0:r, c, :], sq_lo[0:r, g % NS, :],
                                            start=False, stop=False)
                else:
                    pe.wait_ge(lo_ready, TC * t + g + 1)
                    last = nc.tensor.matmul(acc[:, :], w0_hi[0:r, c, :], sq_hi[0:r, g % NS, :],
                                            start=False, stop=True)
                last.then_inc(chunk_used, 1)

            def turn_xk(b):
                pe.wait_ge(xk_copied, b + 1)
                for k in range(GROUPS):
                    last = nc.tensor.transpose(misc[:, k * H:(k + 1) * H], xk[:, k * P:(k + 1) * P], ident[:, :])
                last.then_inc(xk_turned, 1)

            def make_g(b, n, t, first):
                pe.wait_ge(xkt_lo_ready, b + 1)
                pe.wait_ge(spread, 16 * SG * (t + 1))
                if not first or n > 0:
                    pe.wait_ge(g_copied, b)
                for k in range(GROUPS):
                    o = gp[:, k, 0:SG * GI].rearrange("h (e i) -> h e i", e=SG)
                    x_hi = xdiag[:, GROUPS * n + k, :, 0:GI]
                    x_lo = xdiag[:, GROUPS * n + k, :, GI:2 * GI]
                    nc.tensor.matmul(o, xkt_hi[:, k, :], x_hi, start=True, stop=False)
                    nc.tensor.matmul(o, xkt_lo[:, k, :], x_hi, start=False, stop=False)
                    last = nc.tensor.matmul(o, xkt_hi[:, k, :], x_lo, start=False, stop=True)
                last.then_inc(g_ready, 1)

            def make_z2(t):
                pe.wait_ge(g_copied, BLOCKS * (t + 1))
                for i in range(M):
                    last = nc.tensor.matmul(misc[:, 0:P], w1_sb[:, i, :], gs[:, i, :],
                                            start=(i == 0), stop=(i == M - 1))
                last.then_inc(z2_ready, 1)

            def hidden1(t):
                pe.wait_ge(z_copied, t + 1)
                for m in range(H1C):
                    o, c = misc[:, m * P:(m + 1) * P], slice(m * P, (m + 1) * P)
                    nc.tensor.matmul(o, wt1_sb[:, 0, c], zt[:, 0, :], start=True, stop=False)
                    nc.tensor.matmul(o, wt1_sb[:, 1, c], zt[:, 1, :], start=False, stop=False)
                    last = nc.tensor.matmul(o, wt1d_sb[:, c], dense_sb[:, bass.ts(t, P)], start=False, stop=True)
                last.then_inc(h1_ready, 1)

            def hidden2(t):
                pe.wait_ge(h1_done, t + 1)
                for m in range(H2C):
                    for k in range(H1C):
                        last = nc.tensor.matmul(misc[:, m * P:(m + 1) * P], wt2_sb[:, k, m * P:(m + 1) * P],
                                                hid1[:, k, :], start=(k == 0), stop=(k == H1C - 1))
                last.then_inc(h2_ready, 1)

            def make_y(t):
                pe.wait_ge(h2_done, t + 1)
                for k in range(H2C):
                    last = nc.tensor.matmul(misc[0:1, 0:P], wt3_sb[:, k:k + 1], hid2[:, k, :],
                                            start=(k == 0), stop=(k == H2C - 1))
                last.then_inc(y_ready, 1)

            def tile(t, first):
                if not first:
                    turn_xk(BLOCKS * t - 1)
                    pe.wait_ge(hi_by_act, ACT_TILE * t)
                    pe.wait_ge(squared, TC * t)
                pe.wait_ge(emb_split, t + 1)
                for m in range(3):
                    turn_emb(t, m)
                if not first:
                    make_g(BLOCKS * t - 1, BLOCKS - 1, t - 1, False)
                pe.wait_ge(xt_by_dve, 2 * t + 1)
                turn_emb(t, 3)
                pe.wait_ge(xt_by_dve, 2 * (t + 1))
                pe.wait_ge(xt_by_act, 2 * (t + 1))
                pair_sums(t, first, 0)
                for g in range(TC):
                    n, c = divmod(g, CHUNKS)
                    b = BLOCKS * t + n
                    if g + 1 < TC:
                        pair_sums(t, first, g + 1)
                    layer1(t, first, g)
                    if c == 2 and n > 0:
                        if not first:
                            pe.wait_ge((h1_done, h2_done, y_copied)[n - 1], t)
                        turn_xk(b - 1)
                    if c == 3 and n == 0 and not first:
                        pe.wait_ge(xkt_lo_ready, BLOCKS * t)
                        make_z2(t - 1)
                    if c == LAST:
                        if n > 0:
                            make_g(b - 1, n - 1, t, first)
                        if n < 3 and not first:
                            (hidden1, hidden2, make_y)[n](t - 1)

            pe.wait_ge(w0_ready, 3)
            pe.wait_ge(w1_in, 16)
            pe.wait_ge(mlp_in, 7 * 16)
            tile(0, True)
            with pe.Fori(1, TILES) as t:
                tile(t, False)
            last_block = BLOCKS * TILES - 1
            turn_xk(last_block)
            make_g(last_block, BLOCKS - 1, TILES - 1, False)
            make_z2(TILES - 1)
            hidden1(TILES - 1)
            hidden2(TILES - 1)
            make_y(TILES - 1)


def pair_table():
    pairs = [(i, (i + k) % M) for k in range((M + 1) // 2) for i in range(M)]
    rows = -np.ones((CHUNKS, P, 2), np.int64)
    rows[:LAST] = np.array(pairs[:LAST * P]).reshape(LAST, P, 2)
    for at in (AT_HH, AT_HL, AT_LH):
        rows[LAST, at:at + REST] = pairs[LAST * P:]
    return rows


def constants():
    rows = pair_table()
    sel = np.zeros((ROWS, CHUNKS, P), np.float32)
    inc = np.zeros((P, CHUNKS, M), np.float32)
    for c in range(CHUNKS):
        for p in range(P):
            i, j = rows[c, p]
            if i < 0:
                continue
            for part in (0, GI):
                sel[part + i, c, p] += 1.0
                sel[part + j, c, p] += 1.0
            inc[p, c, i] = inc[p, c, j] = 0.125 if i == j else -0.125
    return sel.reshape(ROWS, CHUNKS * P), inc, np.eye(P, dtype=np.float32)


def kernel(**inputs):
    import concourse.bacc as bacc
    from concourse.bass_utils import run_bass_kernel_spmd

    a = {k: np.asarray(v) for k, v in inputs.items()}
    i, j = np.moveaxis(np.maximum(pair_table(), 0), 2, 0)
    w0_rows = a["L0_rec_W0"][0]
    sel, inc, ident = constants()
    arrays = {f"tbl_{f}": np.ascontiguousarray(a[f"tbl_{f}"]) for f in range(M)}
    arrays.update({name: np.ascontiguousarray(x) for name, x in dict(
        ids=a["ids"].reshape(TILES, P, M).transpose(1, 0, 2).reshape(P, TILES * M),
        dense_t=a["dense_ctx"].T,
        w0_pairs=np.stack([w0_rows[i * M + j], w0_rows[j * M + i]]).transpose(0, 2, 1, 3),
        w1=a["L0_rec_W1"].reshape(M, H, H).transpose(1, 0, 2),
        wt1=a["W_top1"], bt1=a["b_top1"].reshape(H1C, P).T,
        wt2=a["W_top2"], bt2=a["b_top2"].reshape(H2C, P).T,
        wt3=a["W_top3"].reshape(H2C, P).T,
        sel=sel, inc=inc, ident=ident).items()})

    nc = bacc.Bacc("TRN2", target_bir_lowering=False, num_devices=1)
    ap = {name: nc.dram_tensor("in_" + name, x.shape, mybir.dt.from_np(x.dtype), kind="ExternalInput").ap()
          for name, x in arrays.items()}
    out = nc.dram_tensor("out", (1, B), F32, kind="ExternalOutput").ap()
    build(nc, [ap[f"tbl_{f}"] for f in range(M)], ap["ids"], ap["dense_t"], ap["w0_pairs"], ap["w1"],
          ap["wt1"], ap["bt1"], ap["wt2"], ap["bt2"], ap["wt3"], ap["sel"], ap["inc"], ap["ident"], out)
    r = run_bass_kernel_spmd(nc, [{"in_" + name: x for name, x in arrays.items()}], core_ids=[0])
    return np.asarray(r.results[0]["out"]).reshape(B, 1)
```
